# Optimizing a Trainium2 kernel written in Bass

```python
import numpy as np
import jax
import jax.numpy as jnp

def _softmax(x, axis=-1):
    return jax.nn.softmax(x, axis=axis)

def _gelu(x):
    return jax.nn.gelu(x, approximate=True)

def _silu(x):
    return jax.nn.silu(x)

def _sigmoid(x):
    return jax.nn.sigmoid(x)

def _layernorm(x, axis=-1, eps=1e-05):
    m = jnp.mean(x, axis=axis, keepdims=True)
    v = jnp.var(x, axis=axis, keepdims=True)
    return (x - m) / jnp.sqrt(v + eps)

def _scatter_add(tgt, idx, src, axis=0):
    return tgt.at[idx].add(src)

def _segment_sum(src, seg, n):
    return jax.ops.segment_sum(src, seg, n)
kernel_name = 'mk_prb_d1_jaxref_r8_e04012'

def setup_inputs(seed: int=0):
    np.random.seed(seed)
    _w = jnp.asarray

    def _L0_attn_setup():
        import jax, jax.numpy as jnp
        import numpy as np
        import math
        B, T, C = (4, 256, 128)
        N_HEAD = 16
        HEAD_DIM = C // N_HEAD
        key = jax.random.key(seed)
        k1, k2, k3, k4, k5 = jax.random.split(key, 5)
        s = 1.0 / math.sqrt(C)
        return {'x': jax.random.normal(k1, (B, T, C), dtype=jnp.float32), 'W_attn': jax.random.normal(k2, (3 * C, C), dtype=jnp.float32) * s, 'b_attn': jax.random.normal(k3, (3 * C,), dtype=jnp.float32) * 0.02, 'W_proj': jax.random.normal(k4, (C, C), dtype=jnp.float32) * s, 'b_proj': jax.random.normal(k5, (C,), dtype=jnp.float32) * 0.02}
    _L0_attn_in = _L0_attn_setup()

    def _L0_ffn_setup():
        import jax, jax.numpy as jnp
        import numpy as np
        N_EXPERT_CAPACITY = 2
        key = jax.random.key(seed)
        k1, k2, k3, k4 = jax.random.split(key, 4)
        B, S, D, E, F = (8, 128, 128, 8, 256)
        x = jax.random.normal(k1, (B, S, D), dtype=jnp.float32)
        choice_w = jax.random.uniform(k2, (E, D), dtype=jnp.float32, minval=-1.0, maxval=1.0) * (1.0 / np.sqrt(D))
        w1 = jax.random.uniform(k3, (E, D, F), dtype=jnp.float32, minval=-1.0, maxval=1.0) * (1.0 / np.sqrt(D))
        w2 = jax.random.uniform(k4, (E, F, D), dtype=jnp.float32, minval=-1.0, maxval=1.0) * (1.0 / np.sqrt(F))
        return {'x': x, 'choice_w': choice_w, 'w1': w1, 'w2': w2}
    _L0_ffn_in = _L0_ffn_setup()
    _d = {'L0_attn_x': _L0_attn_in['x'], 'L0_attn_W_attn': _L0_attn_in['W_attn'], 'L0_attn_b_attn': _L0_attn_in['b_attn'], 'L0_attn_W_proj': _L0_attn_in['W_proj'], 'L0_attn_b_proj': _L0_attn_in['b_proj'], 'L0_ffn_choice_w': _L0_ffn_in['choice_w'], 'L0_ffn_w1': _L0_ffn_in['w1'], 'L0_ffn_w2': _L0_ffn_in['w2']}
    _x0 = _d['L0_attn_x']
    _d['L0_attn_x'] = jax.random.normal(jax.random.fold_in(jax.random.key(seed), 1), (1, 2048, 128), dtype=_x0.dtype)
    del _x0
    return _d

def reference(L0_attn_x, L0_attn_W_attn, L0_attn_b_attn, L0_attn_W_proj, L0_attn_b_proj, L0_ffn_choice_w, L0_ffn_w1, L0_ffn_w2):

    def _L0_attn_ref(x, W_attn, b_attn, W_proj, b_proj):
        import jax, jax.numpy as jnp
        import numpy as np
        import math
        B, T, C = (4, 256, 128)
        N_HEAD = 16
        HEAD_DIM = C // N_HEAD
        Bx, Tx, Cx = x.shape
        qkv = jnp.einsum('btc,dc->btd', x, W_attn) + b_attn
        q, k, v = jnp.split(qkv, 3, axis=-1)

        def to_heads(t):
            return t.reshape(Bx, Tx, N_HEAD, HEAD_DIM).transpose(0, 2, 1, 3)
        q, k, v = (to_heads(q), to_heads(k), to_heads(v))
        scale = 1.0 / math.sqrt(HEAD_DIM)
        att = jnp.einsum('bhqd,bhkd->bhqk', q, k) * scale
        causal = jnp.tril(jnp.ones((Tx, Tx), dtype=bool))
        att = jnp.where(causal, att, -jnp.inf)
        att = jax.nn.softmax(att, axis=-1)
        y = jnp.einsum('bhqk,bhkd->bhqd', att, v)
        y = y.transpose(0, 2, 1, 3).reshape(Bx, Tx, Cx)
        y = jnp.einsum('btc,dc->btd', y, W_proj) + b_proj
        return y

    def _L0_ffn_ref(x, choice_w, w1, w2):
        import jax, jax.numpy as jnp
        import numpy as np
        N_EXPERT_CAPACITY = 2
        B, S, D = x.shape
        E = choice_w.shape[0]
        k = S * N_EXPERT_CAPACITY // E
        probs = jax.nn.softmax(jnp.einsum('bsd,ed->bse', x, choice_w), axis=-1)
        G, I = jax.lax.top_k(jnp.swapaxes(probs, -1, -2), k)
        x_in = jnp.take_along_axis(x[:, None, :, :], I[..., None], axis=2)
        h = jax.nn.silu(jnp.einsum('bekd,edf->bekf', x_in, w1))
        x_mlp = jnp.einsum('bekf,efd->bekd', h, w2)
        b_idx = jnp.arange(B)[:, None, None]
        out = jnp.zeros_like(x).at[b_idx, I].add(G[..., None] * x_mlp)
        return out
    x = L0_attn_x
    xn = _layernorm(x, axis=-1)
    x = x + _L0_attn_ref(xn, L0_attn_W_attn, L0_attn_b_attn, L0_attn_W_proj, L0_attn_b_proj) + _L0_ffn_ref(xn, L0_ffn_choice_w, L0_ffn_w1, L0_ffn_w2)
    return x

_drawn_inputs = setup_inputs


def setup_inputs(seed=0):
    import zlib

    import numpy as np

    out = dict(_drawn_inputs(seed))
    spreads = {}
    factors = {'L0_attn_b_proj': 3.02}
    for name, (base, spread) in spreads.items():
        noise = np.random.default_rng([zlib.crc32(name.encode()), seed]).standard_normal(out[name].shape)
        drawn = base * np.exp(spread * noise) if base else spread * noise
        out[name] = jnp.asarray(drawn.astype(out[name].dtype))
    for name, factor in factors.items():
        out[name] = (out[name] * factor).astype(out[name].dtype)
    return out
```

```python
from contextlib import ExitStack

import concourse.bass as bass
from concourse import mybir

F32 = mybir.dt.float32
BF16 = mybir.dt.bfloat16
I32 = mybir.dt.int32
ALU = mybir.AluOpType
ACT = mybir.ActivationFunctionType
AX = mybir.AxisListType


def block_kernel(nc, x, w_attn, b_attn, w_proj, b_proj, choice_w, w1, w2, out):
    T, C = x.shape[1], x.shape[2]
    P = 128
    NT = T // P
    H = 16
    D = C // H
    E, F = choice_w.shape[0], w1.shape[2]
    FH = F // P
    TOPK = T * 2 // E
    N = 512
    NC = T // N
    TPC = N // P
    HG = 4
    G = H // HG
    SCALE = 1.0 / float(D) ** 0.5
    EPS = 1e-5
    BITS = 30
    INF = 3.0e38
    BOUND_LIMIT = 35.0 / SCALE / 1.02

    K_PART = [0, 0, 0, 1, 1, 2]
    Q_PART = [0, 1, 2, 0, 1, 0]
    ROWS = D * len(K_PART)
    NSH = 3
    KR = ROWS + NSH

    STEPS = [(c, j) for c in range(NC) for j in range(TPC * (c + 1))]
    NS = len(STEPS)
    NU = 2 * NS
    SB = 3
    PB = 4
    LEAD = SB
    LAST_OF_CHUNK = [2 * STEPS.index((c, TPC * (c + 1) - 1)) + 1 for c in range(NC)]
    LAST_OF_KEYS = [2 * STEPS.index((NC - 1, TPC * (c + 1) - 1)) + 1 for c in range(NC)]

    ctx = ExitStack()
    with ctx:
        def sb(name, shape, dt=F32):
            return ctx.enter_context(nc.sbuf_tensor(name, shape, dt))

        def sem(name):
            return ctx.enter_context(nc.semaphore(name))

        x_sb = sb("x_sb", [P, NT, C])
        xn = sb("xn", [P, NT, C])
        xnT = sb("xnT", [P, T])
        stats = sb("stats", [P, NT, 6])
        mv = sb("mv", [P, NT, 2])
        rstd = sb("rstd", [P, NT])
        ident = sb("ident", [P, P])
        w_rows = sb("w_rows", [P, 4, C])
        cw_rows = sb("cw_rows", [E, C])
        wT = sb("wT", [P, 4, C])
        cwT = sb("cwT", [P, E])
        b_qk = sb("b_qk", [P, 2])
        b_v = sb("b_v", [P, C])
        b_o = sb("b_o", [P, C])
        qT = sb("qT", [P, T])
        kT = sb("kT", [P, T])
        parts = sb("parts", [P, 2, 3, T], BF16)
        v_all = sb("v_all", [P, NT, C])
        v_grp = sb("v_grp", [P, NT, HG, 32])
        k_aug = sb("k_aug", [2 * KR, 2, T], BF16)
        q_aug = sb("q_aug", [2 * KR, HG, T], BF16)
        ones_rows = sb("ones_rows", [H * NSH, N], BF16)
        zero_rows = sb("zero_rows", [H * (NSH - 1), N], BF16)
        future = sb("future", [P, P])
        flag_max = sb("flag_max", [H, 2])
        flag = sb("flag", [H, 1], I32)
        row_max = sb("row_max", [P, HG * NT])
        half_max = sb("half_max", [P, 2])
        row_shift = sb("row_shift", [P, NSH, HG * NT], BF16)
        head_sel = sb("head_sel", [P, H], BF16)
        shift = sb("shift", [H, T], BF16)
        sq = sb("sq", [P, N], BF16)
        kk_max = sb("kk_max", [H, NT])
        m_bound = sb("m_bound", [H, T])
        causal = sb("causal", [P, P])
        probs = sb("probs", [P, PB, HG, N])
        y_acc = sb("y_acc", [P, 2, N])
        y_num, y_den = qT, kT
        gate = sb("gate", [P, NT, E])
        g_red = sb("g_red", [P, NT])
        r_p = sb("r_p", [P, NT, E])
        thr = sb("thr", [P, E])
        cand = sb("cand", [P, E])
        bits = sb("bits", [P, BITS, E])
        ge = sb("ge", [P, NT, E])
        cnt = sb("cnt", [P, E])
        tot = sb("tot", [P, E])
        tri = sb("tri", [P, P], BF16)
        ones_pp = sb("ones_pp", [P, P], BF16)
        eq = sb("eq", [P, NT, E], BF16)
        gt = sb("gt", [P, NT, E])
        gt_n = sb("gt_n", [P, E], BF16)
        eq_rank = sb("eq_rank", [P, NT, E])
        eq_tot = sb("eq_tot", [P, NT + 1, E])
        w1_sb = sb("w1_sb", [P, E, F])
        w2_sb = sb("w2_sb", [P, E, FH, C])
        th = sb("th", [P, 2, N])
        hT = sb("hT", [P, 2, FH, N])
        moe = xn

        bank = [ctx.enter_context(nc.psum_tensor(f"bank{i}", [P, 2, N], F32)) for i in range(4)]
        scores = bank[:SB]
        acc = bank[3][:, 0]
        spare = bank[3][:, 1]

        qk_dram = nc.dram_tensor("qk_dram", [2, G, HG, KR, T], BF16, kind="Internal").ap()
        y_dram = nc.dram_tensor("y_dram", [G, HG, 2 * D, T], F32, kind="Internal").ap()

        qk_flat = qk_dram.rearrange("s g h r t -> s (g h) r t")
        y_flat = y_dram.rearrange("g h r t -> (g h) r t")

        s_x = [sem(f"x_loaded{c}") for c in range(NC)]
        s_w = sem("weights_loaded")
        s_bias = sem("biases_loaded")
        s_moe_w = sem("moe_weights_loaded")
        s_ident = sem("ident_ready")
        s_const = sem("constants_ready")
        s_pool = sem("pool_step")
        s_turn = sem("pool_turn")
        s_fmax = sem("bound_max_ready")
        s_fall = sem("bound_max_shared")
        s_flag = sem("bounds_judged")
        s_gstage = sem("raw_group_staged")
        s_gscore = sem("raw_scores_ready")
        s_gread = sem("raw_scores_read")
        s_gstep = sem("raw_row_step")
        s_gpart = sem("row_shift_part")
        s_gshift = sem("row_shifts_ready")
        s_gsent = sem("row_shifts_sent")
        s_dve = sem("vector_step")
        s_var = sem("variances_ready")
        s_std = sem("std_ready")
        s_xn = sem("xn_ready")
        s_wt_ps = sem("weights_transposed")
        s_wt = sem("weights_T_ready")
        s_xt_ps = sem("xn_transposed")
        s_xt = sem("xnT_ready")
        s_qkv_ps = sem("qkv_product")
        s_q = sem("q_ready")
        s_k = sem("k_ready")
        s_v = sem("v_ready")
        s_logit = sem("logits_product")
        s_lmax = sem("logits_centred")
        s_lexp = sem("logits_exp")
        s_rp = sem("router_probs_ready")
        s_sq = sem("squares_ready")
        s_norm = sem("norms_product")
        s_mm = sem("bound_squared_ready")
        s_mb = sem("bound_ready")
        s_shift = sem("shift_ready")
        s_cast = sem("part_cast")
        s_rem = sem("part_remainder")
        s_dram = sem("qk_in_dram")
        s_stage_q = [sem(f"q_staged{c}") for c in range(NC)]
        s_stage_k = [sem(f"k_staged{c}") for c in range(NC)]
        s_sready = sem("scores_ready")
        s_exp = sem("probs_ready")
        s_mask = sem("causal_masked")
        s_pfree = sem("probs_used")
        s_vgrp = sem("group_values_ready")
        s_acc = sem("chunk_summed")
        s_accfree = sem("chunk_sum_copied")
        s_ysent = [sem(f"y_sent{b}") for b in range(2)]
        s_thr = sem("thresholds_ready")
        s_eq = sem("ties_marked")
        s_rank = sem("ties_ranked")
        s_gate = sem("gates_ready")
        s_yload = [sem(f"y_loaded{c}") for c in range(NC)]
        s_y = sem("y_ready")
        s_att = sem("projection_ready")
        s_attread = sem("projection_read")
        s_h = sem("hidden_product")
        s_th = sem("tanh_ready")
        s_ha = sem("hidden_ready")
        s_mo = sem("expert_product")
        s_moread = sem("expert_product_read")
        s_out = sem("output_tile_ready")
        s_done = sem("output_stored")

        def flat(i):
            return bank[i // 2][:, i % 2, :]

        def before(u):
            if u >= SB:
                return u - SB + 1
            return max(v for v in range(NU) if v % SB == u) + 1 - NU

        block = ctx.enter_context(nc.Block())

        def stage_q(sp, g, c, rows=KR):
            for h in reversed(range(HG)):
                sp.dma_start(q_aug[KR * (h % 2):KR * (h % 2) + rows, h, c * N:(c + 1) * N],
                             qk_dram[1, bass.ds(g, 1), h, 0:rows, c * N:(c + 1) * N]).then_inc(s_stage_q[c], 16)

        def stage_k(sp, g, c):
            for p in reversed(range(2)):
                src = qk_dram[0, bass.ds(g, 1), 2 * p:2 * p + 2, :, c * N:(c + 1) * N]
                sp.dma_start(k_aug[:, p, c * N:(c + 1) * N], src.rearrange("g a r t -> (g a r) t"))\
                  .then_inc(s_stage_k[c], 16)

        @block.sync
        def _(sp):
            x_t = x[0].rearrange("(n p) c -> p n c", p=P)
            for c in range(NC):
                sp.dma_start(x_sb[:, TPC * c:TPC * (c + 1), :], x_t[:, TPC * c:TPC * (c + 1), :])\
                  .then_inc(s_x[c], 16)
            sp.dma_start(w_rows[:, 0:3, :], w_attn.rearrange("(i p) c -> p i c", p=P)).then_inc(s_w, 16)
            sp.dma_start(w_rows[:, 3, :], w_proj).then_inc(s_w, 16)
            sp.dma_start(cw_rows[:, :], choice_w).then_inc(s_w, 16)
            with nc.allow_non_contiguous_dma("a bias per partition"):
                sp.dma_start(b_qk[:, :], b_attn[0:2 * C].rearrange("(i p) -> p i", p=P)).then_inc(s_bias, 16)
            sp.dma_start(b_v[:, :], b_attn[2 * C:3 * C].partition_broadcast(P)).then_inc(s_bias, 16)
            sp.dma_start(b_o[:, :], b_proj.partition_broadcast(P)).then_inc(s_bias, 16)
            sp.dma_start(w1_sb[:, :, :], w1.rearrange("e c f -> c e f")).then_inc(s_moe_w, 16)
            sp.dma_start(w2_sb[:, :, :, :], w2.rearrange("e (i p) c -> p e i c", p=P)).then_inc(s_moe_w, 16)
            sp.wait_ge(s_const, 3)
            for c in range(NC):
                cs = slice(c * N, (c + 1) * N)
                sp.dma_start(qk_flat[0, :, ROWS:KR, cs], ones_rows[:, :]).then_inc(s_dram, 16)
                sp.dma_start(qk_flat[1, :, ROWS + 1:KR, cs], zero_rows[:, :]).then_inc(s_dram, 16)
            sp.wait_ge(s_shift, 1)
            sp.dma_start(qk_flat[1, :, ROWS, :], shift[:, :]).then_inc(s_dram, 16)
            n = 2 * NC + 1
            for part in range(3):
                for side, used in enumerate((K_PART, Q_PART)):
                    sp.wait_ge(s_cast, 2 * part + side + 1)
                    for r in range(len(used)):
                        if used[r] == part:
                            sp.dma_start(qk_flat[side, :, D * r:D * (r + 1), :], parts[:, side, part, :])\
                              .then_inc(s_dram, 16)
                            n += 1
            sp.wait_ge(s_dram, 16 * n)

            sp.wait_ge(s_flag, 1)
            loose = sp.value_load(flag[0:1, 0:1], min_val=0, max_val=1)
            with sp.If(loose > 0):
                with sp.Fori(0, G) as g:
                    sp.wait_ge(s_gsent, 16 * NSH * HG * g + 1)
                    for h in reversed(range(HG)):
                        sp.dma_start(q_aug[KR * (h % 2):KR * (h % 2) + ROWS, h, :],
                                     qk_dram[1, bass.ds(g, 1), h, 0:ROWS, :]).then_inc(s_gstage, 16)
                    for p in reversed(range(2)):
                        src = qk_dram[0, bass.ds(g, 1), 2 * p:2 * p + 2, :, :]
                        sp.dma_start(k_aug[:, p, :], src.rearrange("g a r t -> (g a r) t")).then_inc(s_gstage, 16)
                    sp.wait_ge(s_gshift, g + 1)
                    with nc.allow_non_contiguous_dma("a query's shift from its partition into a row"):
                        for h in reversed(range(HG)):
                            for i in reversed(range(NSH)):
                                dst = qk_dram[1, bass.ds(g, 1), h, ROWS + i, :].rearrange("g (n p) -> p (g n)", p=P)
                                sp.dma_start(dst, row_shift[:, i, h * NT:(h + 1) * NT]).then_inc(s_gsent, 16)
                sp.wait_ge(s_gsent, 16 * NSH * HG * G + 1)
            for c in range(NC):
                stage_q(sp, 0, c)
                stage_k(sp, 0, c)

            def group(g, last):
                def send_y(c):
                    sp.wait_ge(s_accfree, NC * g + c + 2)
                    for h in reversed(range(HG)):
                        sp.dma_start(y_dram[bass.ds(g, 1), h, :, c * N:(c + 1) * N],
                                     y_acc[32 * h:32 * h + 2 * D, c % 2, :]).then_inc(s_ysent[c % 2], 16)

                for c in range(NC - 1):
                    if not last:
                        sp.wait_ge(s_sready, NU * g + LAST_OF_CHUNK[c] + 1)
                        stage_q(sp, g + 1, c)
                    send_y(c)
                if not last:
                    for c in range(NC):
                        sp.wait_ge(s_sready, NU * g + LAST_OF_KEYS[c] + 1)
                        stage_k(sp, g + 1, c)
                    sp.wait_ge(s_sready, NU * g + NU)
                    stage_q(sp, g + 1, NC - 1)
                send_y(NC - 1)

            with sp.Fori(0, G - 1) as g:
                group(g, False)
            group(G - 1, True)
            for b in range(2):
                sp.wait_ge(s_ysent[b], 16 * HG * G * NC // 2 + 1)
            for c in range(NC):
                sp.dma_start(y_num[:, c * N:(c + 1) * N], y_flat[:, 0:D, c * N:(c + 1) * N]).then_inc(s_yload[c], 16)
                sp.dma_start(y_den[:, c * N:(c + 1) * N], y_flat[:, D:2 * D, c * N:(c + 1) * N]).then_inc(s_yload[c], 16)
            o_t = out[0].rearrange("(n p) c -> p n c", p=P)
            for c in range(NC):
                sp.wait_ge(s_out, c + 1)
                sp.dma_start(o_t[:, TPC * c:TPC * (c + 1), :], moe[:, TPC * c:TPC * (c + 1), :]).then_inc(s_done, 16)
            sp.wait_ge(s_done, 16 * NC)

        @block.gpsimd
        def _(pool):
            steps = [0]

            def step(ins):
                steps[0] += 1
                ins.then_inc(s_pool, 1)
                pool.wait_ge(s_pool, steps[0])

            step(pool.memset(ident[:, :], 0.0))
            pool.affine_select(out=ident[:, :], in_=ident[:, :], compare_op=ALU.not_equal, fill=1.0, base=0,
                               pattern=[[-1, P]], channel_multiplier=1).then_inc(s_ident, 1)
            pool.memset(q_aug[:, :, :].bitcast(I32), 0).then_inc(s_const, 1)
            pool.memset(ones_rows[:, :], 1.0).then_inc(s_const, 1)
            pool.memset(zero_rows[:, :], 0.0).then_inc(s_const, 1)
            pool.memset(ones_pp[:, :], 1.0).then_inc(s_const, 1)
            pool.memset(v_grp[:, :, :, :], 1.0).then_inc(s_const, 1)
            step(pool.memset(head_sel[:, :], 1.0))
            step(pool.affine_select(out=head_sel[:, :], in_=head_sel[:, :], compare_op=ALU.is_ge, fill=0.0, base=0,
                                    pattern=[[-D, H]], channel_multiplier=1))
            pool.affine_select(out=head_sel[:, :], in_=head_sel[:, :], compare_op=ALU.is_ge, fill=0.0, base=D - 1,
                               pattern=[[D, H]], channel_multiplier=-1).then_inc(s_const, 1)
            step(pool.memset(causal[:, :], INF))
            pool.affine_select(out=causal[:, :], in_=causal[:, :], compare_op=ALU.is_ge, fill=0.0, base=0,
                               pattern=[[1, P]], channel_multiplier=-1).then_inc(s_const, 1)
            step(pool.memset(future[:, :], 0.0))
            pool.affine_select(out=future[:, :], in_=future[:, :], compare_op=ALU.is_ge, fill=-INF, base=0,
                               pattern=[[-1, P]], channel_multiplier=1).then_inc(s_const, 1)
            step(pool.memset(tri[:, :], 1.0))
            pool.affine_select(out=tri[:, :], in_=tri[:, :], compare_op=ALU.is_gt, fill=0.0, base=0,
                               pattern=[[1, P]], channel_multiplier=-1).then_inc(s_const, 1)
            for b in range(BITS):
                last = pool.memset(bits[:, b, :].bitcast(I32), 1 << (BITS - 1 - b))
            step(last)
            step(pool.memset(thr[:, :].bitcast(I32), 0))
            pool.wait_ge(s_fmax, 1)
            pool.partition_all_reduce(flag_max[:, 1:2], flag_max[:, 0:1], H, bass.bass_isa.ReduceOp.max).then_inc(s_fall, 1)
            pool.wait_ge(s_rp, 1)
            with pool.Fori(0, BITS) as b:
                at = [0]

                def turn(ins):
                    at[0] += 1
                    ins.then_inc(s_turn, 1)
                    pool.wait_ge(s_turn, at[0])

                turn(pool.tensor_tensor(cand[:, :].bitcast(I32), thr[:, :].bitcast(I32),
                                        bits[:, bass.ds(b, 1), :].rearrange("p a e -> p (a e)").bitcast(I32), ALU.add))
                turn(pool.tensor_tensor(ge[:, :, :], r_p[:, :, :],
                                        cand[:, :].unsqueeze(1).broadcast_to([P, NT, E]), ALU.subtract))
                turn(pool.tensor_scalar(ge[:, :, :], ge[:, :, :], 0.0, None, ALU.is_ge))
                w = NT // 2
                while w >= 1:
                    turn(pool.tensor_tensor(ge[:, 0:w, :], ge[:, 0:w, :], ge[:, w:2 * w, :], ALU.add))
                    w //= 2
                turn(pool.partition_all_reduce(tot[:, :], ge[:, 0, :], P, bass.bass_isa.ReduceOp.add))
                turn(pool.tensor_scalar(tot[:, :], tot[:, :], TOPK - 0.5, None, ALU.is_ge))
                turn(pool.tensor_tensor(cand[:, :], cand[:, :], thr[:, :], ALU.subtract))
                turn(pool.tensor_tensor(cand[:, :], cand[:, :], tot[:, :], ALU.mult))
                turn(pool.tensor_tensor(thr[:, :], thr[:, :], cand[:, :], ALU.add))
                pool.sem_clear(s_turn)
            pool.memset(cnt[:, :], 0.0).then_inc(s_thr, 1)

        @block.scalar
        def _(act):
            act.wait_ge(s_var, 1)
            act.activation(rstd[:, :], mv[:, :, 1], ACT.Sqrt, bias=EPS).then_inc(s_std, 1)
            for c in range(NC):
                act.wait_ge(s_xt_ps, c + 1)
                act.activation(xnT[:, c * N:(c + 1) * N], flat(6 + c % 2), ACT.Copy).then_inc(s_xt, 1)
            act.wait_ge(s_bias, 48)
            for c in range(NC):
                act.wait_ge(s_qkv_ps, c + 1)
                act.activation(qT[:, c * N:(c + 1) * N], flat(3 * (c % 2)), ACT.Identity, bias=b_qk[:, 0:1])\
                   .then_inc(s_q, 1)
            for i in range(2 * NC):
                src, ready = ((kT, s_k) if i < NC else (qT, s_q))
                c = i % NC
                act.wait_ge(ready, c + 1)
                if i >= 1:
                    act.wait_ge(s_norm, i)
                act.activation(sq[:, :], src[:, c * N:(c + 1) * N], ACT.Square).then_inc(s_sq, 1)
            for c in range(NC):
                act.wait_ge(s_mm, c + 1)
                act.activation(m_bound[:, c * N:(c + 1) * N], m_bound[:, c * N:(c + 1) * N], ACT.Sqrt)\
                   .then_inc(s_mb, 1)
            act.wait_ge(s_lmax, 1)
            act.activation(r_p[:, :, :], r_p[:, :, :], ACT.Exp).then_inc(s_lexp, 1)

            for part in range(3):
                for side, src in enumerate((kT, qT)):
                    act.wait_ge(s_rem, 2 * part + side + 1)
                    act.activation(parts[:, side, part, :], src[:, :], ACT.Copy).then_inc(s_cast, 1)

            act.sem_inc(s_exp, SB)
            act.sem_inc(s_pfree, 1)

            def group(g):
                for u in range(NU):
                    c, j = STEPS[u // 2]
                    off = max(0, j - TPC * c) * P
                    p = u % 2
                    act.wait_ge(s_sready, NU * g + u + 1)
                    if p == 0 and u // 2 < PB:
                        act.wait_ge(s_pfree, NS * g + 1)
                    elif p == 0:
                        act.wait_ge(s_pfree, NS * g + u // 2 - PB + 2)
                    act.activation(probs[:, (u // 2) % PB, 2 * p:2 * p + 2, off:N],
                                   scores[u % SB][:, :, off:N], ACT.Exp, scale=SCALE).then_inc(s_exp, 1)

            with act.Fori(0, G) as g:
                group(g)

            for i in range(E * NC):
                for f in range(FH):
                    act.wait_ge(s_h, FH * i + f + 1)
                    if i >= 1:
                        act.wait_ge(s_ha, FH * (i - 1) + f + 1)
                    act.activation(th[:, f, :], bank[i % 2][:, f, :], ACT.Tanh, scale=0.5).then_inc(s_th, 1)

        @block.vector
        def _(dve):
            chain = [0]

            def link(ins):
                chain[0] += 1
                ins.then_inc(s_dve, 1)
                dve.wait_ge(s_dve, chain[0])

            for n in range(NT):
                if n % TPC == 0:
                    dve.wait_ge(s_x[n // TPC], 16)
                last = dve.bn_stats(stats[:, n, :], x_sb[:, n, :])
            link(last)
            for n in range(NT):
                last = dve.bn_aggr(mv[:, n, :], stats[:, n, :])
            last.then_inc(s_var, 1)
            dve.wait_ge(s_std, 1)
            link(dve.reciprocal(rstd[:, :], rstd[:, :]))
            for n in range(NT):
                last = dve.tensor_scalar(xn[:, n, :], x_sb[:, n, :], mv[:, n, 0:1], rstd[:, n:n + 1],
                                         ALU.subtract, ALU.mult)
                if n % TPC == TPC - 1:
                    last.then_inc(s_xn, 1)
            dve.wait_ge(s_wt_ps, 1)
            dve.tensor_copy(wT[:, :, :], flat(0).rearrange("p (i c) -> p i c", i=4)).then_inc(s_wt, 1)
            dve.tensor_copy(cwT[:, :], flat(1)[:, 0:E]).then_inc(s_wt, 1)
            dve.wait_ge(s_bias, 48)
            for c in range(NC):
                dve.wait_ge(s_qkv_ps, c + 1)
                dve.tensor_scalar(kT[:, c * N:(c + 1) * N], flat(3 * (c % 2) + 1), b_qk[:, 1:2], None, ALU.add)\
                   .then_inc(s_k, 1)
                dve.tensor_tensor(v_all[:, TPC * c:TPC * (c + 1), :],
                                  flat(3 * (c % 2) + 2).rearrange("p (n c) -> p n c", n=TPC),
                                  b_v[:, :].unsqueeze(1).broadcast_to([P, TPC, C]), ALU.add).then_inc(s_v, 1)
            dve.wait_ge(s_logit, 1)
            logits = flat(7)[:, 0:NT * E].rearrange("p (n e) -> p n e", e=E)
            link(dve.reduce_max(g_red[:, :], logits, AX.X))
            dve.tensor_tensor(r_p[:, :, :], logits, g_red[:, :].unsqueeze(2).broadcast_to([P, NT, E]),
                              ALU.subtract).then_inc(s_lmax, 1)
            for c in range(NC):
                dve.wait_ge(s_norm, c + 1)
                last = dve.reduce_max(kk_max[:, TPC * c:TPC * (c + 1)],
                                      flat(c)[0:H, :].rearrange("h (n p) -> h n p", n=TPC), AX.X)
            link(last)
            for n in range(1, NT):
                link(dve.tensor_tensor(kk_max[:, n:n + 1], kk_max[:, n:n + 1], kk_max[:, n - 1:n], ALU.max))
            for c in range(NC):
                dve.wait_ge(s_norm, NC + c + 1)
                tiles = "h (n p) -> h n p"
                dve.tensor_tensor(m_bound[:, c * N:(c + 1) * N].rearrange(tiles, n=TPC),
                                  flat(NC + c)[0:H, :].rearrange(tiles, n=TPC),
                                  kk_max[:, TPC * c:TPC * (c + 1)].unsqueeze(2).broadcast_to([H, TPC, P]),
                                  ALU.mult).then_inc(s_mm, 1)
            dve.wait_ge(s_mb, NC)
            dve.tensor_scalar(shift[:, :], m_bound[:, :], -1.02, None, ALU.mult).then_inc(s_shift, 1)
            dve.reduce_max(flag_max[:, 0:1], m_bound[:, :], AX.X).then_inc(s_fmax, 1)
            dve.sem_inc(s_rem, 2)
            for part in range(2):
                for side, src in enumerate((kT, qT)):
                    dve.wait_ge(s_cast, 2 * part + side + 1)
                    dve.tensor_tensor(src[:, :], src[:, :], parts[:, side, part, :], ALU.subtract)\
                       .then_inc(s_rem, 1)
            dve.wait_ge(s_fall, 1)
            dve.tensor_scalar(flag[:, :], flag_max[:, 1:2], BOUND_LIMIT, None, ALU.is_gt).then_inc(s_flag, 1)
            dve.wait_ge(s_lexp, 1)
            link(dve.reduce_sum(g_red[:, :], r_p[:, :, :], AX.X))
            link(dve.reciprocal(g_red[:, :], g_red[:, :]))
            dve.tensor_tensor(r_p[:, :, :], r_p[:, :, :], g_red[:, :].unsqueeze(2).broadcast_to([P, NT, E]),
                              ALU.mult).then_inc(s_rp, 1)
            dve.tensor_tensor(moe[:, :, :], x_sb[:, :, :], b_o[:, :].unsqueeze(1).broadcast_to([P, NT, C]), ALU.add)
            dve.wait_ge(s_v, NC)
            dve.wait_ge(s_const, 8)

            dve.wait_ge(s_flag, 1)
            loose = dve.value_load(flag[0:1, 0:1], min_val=0, max_val=1)
            with dve.If(loose > 0):
                dve.sem_inc(s_gread, 1)
                dve.sem_inc(s_gsent, 1)
                with dve.Fori(0, G) as g:
                    for h in range(HG):
                        for n in range(NT):
                            i = h * NT + n
                            dve.wait_ge(s_gscore, HG * NT * g + i + 1)
                            own = flat(n // TPC)[:, (n % TPC) * P:(n % TPC + 1) * P]
                            dve.tensor_tensor(own, own, future[:, :], ALU.add).then_inc(s_gstep, 1)
                            dve.wait_ge(s_gstep, 2 * (HG * NT * g + i) + 1)
                            width = (n + 1) * P
                            halves = [min(width, 2 * N)] + ([width - 2 * N] if width > 2 * N else [])
                            for b, w in enumerate(halves):
                                row = bank[b][:, :, :].rearrange("p b n -> p (b n)")[:, 0:w]
                                last = dve.reduce_max(half_max[:, b:b + 1], row, AX.X)
                            last.then_inc(s_gstep, 1)
                            dve.wait_ge(s_gstep, 2 * (HG * NT * g + i) + 2)
                            dve.reduce_max(row_max[:, i:i + 1], half_max[:, 0:len(halves)], AX.X).then_inc(s_gread, 1)
                    dve.wait_ge(s_gread, HG * NT * (g + 1) + 1)
                    dve.wait_ge(s_gsent, 16 * NSH * HG * g + 1)
                    dve.tensor_scalar(row_max[:, :], row_max[:, :], -1.0, None, ALU.mult).then_inc(s_gpart, 1)
                    for i in range(NSH):
                        dve.wait_ge(s_gpart, (2 * NSH - 1) * g + 2 * i + 1)
                        part = dve.tensor_copy(row_shift[:, i, :], row_max[:, :])
                        if i == NSH - 1:
                            part.then_inc(s_gshift, 1)
                            break
                        part.then_inc(s_gpart, 1)
                        dve.wait_ge(s_gpart, (2 * NSH - 1) * g + 2 * i + 2)
                        dve.tensor_tensor(row_max[:, :], row_max[:, :], row_shift[:, i, :], ALU.subtract)\
                           .then_inc(s_gpart, 1)
            dve.sem_inc(s_accfree, 1)
            for b in range(2):
                dve.sem_inc(s_ysent[b], 1)

            def group(g):
                src = v_all[:, :, bass.ds(HG * D * g, HG * D)].rearrange("p n (h d) -> p n h d", h=HG)
                dve.tensor_copy(v_grp[:, :, :, 0:D], src).then_inc(s_vgrp, 1)
                for k, (c, j) in enumerate(STEPS):
                    if j >= TPC * c:
                        off = (j - TPC * c) * P
                        dve.wait_ge(s_exp, NU * g + SB + 2 * k + 2)
                        tile = probs[:, k % PB, :, off:off + P]
                        dve.tensor_tensor(tile, tile, causal[:, :].unsqueeze(1).broadcast_to([P, HG, P]),
                                          ALU.min).then_inc(s_mask, 1)
                    if j == TPC * (c + 1) - 1:
                        dve.wait_ge(s_pfree, NS * g + k + 2)
                        dve.wait_ge(s_ysent[c % 2], 16 * HG * (NC // 2) * g + 16 * HG * (c // 2) + 1)
                        dve.tensor_copy(y_acc[:, c % 2, :], acc).then_inc(s_accfree, 1)

            with dve.Fori(0, G) as g:
                group(g)

            dve.wait_ge(s_thr, 1)
            thr_b = thr[:, :].unsqueeze(1).broadcast_to([P, NT, E])
            dve.tensor_tensor(eq[:, :, :], r_p[:, :, :], thr_b, ALU.is_equal)
            link(dve.tensor_tensor(gt[:, :, :], r_p[:, :, :], thr_b, ALU.is_gt))
            with nc.allow_low_precision(reason="counts up to the number of tiles"):
                dve.tensor_reduce(gt_n[:, :], gt[:, :, :].rearrange("p n e -> p e n"), AX.X, ALU.add)\
                   .then_inc(s_eq, 1)
            dve.wait_ge(s_rank, 1)
            ranks = spare[:, 0:NT * E].rearrange("p (n e) -> p n e", e=E)
            totals = spare[:, NT * E:2 * NT * E].rearrange("p (n e) -> p n e", e=E)
            link(dve.memset(eq_tot[:, 0, :], 0.0))
            for n in range(NT):
                link(dve.tensor_tensor(eq_tot[:, n + 1, :], eq_tot[:, n, :], totals[:, n, :], ALU.add))
            link(dve.tensor_tensor(eq_rank[:, :, :], eq_tot[:, 0:NT, :], ranks, ALU.add))
            link(dve.tensor_scalar(cnt[:, :], spare[:, 2 * NT * E:2 * NT * E + E], -1.0, float(TOPK),
                                   ALU.mult, ALU.add))
            link(dve.tensor_tensor(eq_rank[:, :, :], eq_rank[:, :, :],
                                   cnt[:, :].unsqueeze(1).broadcast_to([P, NT, E]), ALU.is_lt))
            link(dve.tensor_tensor(eq_rank[:, :, :], eq_rank[:, :, :], eq[:, :, :], ALU.mult))
            link(dve.tensor_tensor(gt[:, :, :], gt[:, :, :], eq_rank[:, :, :], ALU.add))
            link(dve.scalar_tensor_tensor(out=gate[:, :, :], in0=gt[:, :, :], scalar=0.5, in1=r_p[:, :, :],
                                          op0=ALU.mult, op1=ALU.mult))

            def add_expert(i):
                e, c = i // NC, i % NC
                dve.wait_ge(s_mo, i + 1)
                for t in range(TPC):
                    n = TPC * c + t
                    last = dve.scalar_tensor_tensor(out=moe[:, n, :], in0=bank[2][:, i % 2, t * C:(t + 1) * C],
                                                    scalar=gate[:, n, e:e + 1], in1=moe[:, n, :],
                                                    op0=ALU.mult, op1=ALU.add)
                last.then_inc(s_moread, 1)
                dve.wait_ge(s_moread, i + 1)

            for i in range(E * NC):
                for f in range(FH):
                    dve.wait_ge(s_th, FH * i + f + 1)
                    if i >= 2:
                        dve.wait_ge(s_mo, i - 1)
                    dve.scalar_tensor_tensor(out=hT[:, i % 2, f, :], in0=th[:, f, :], scalar=1.0,
                                             in1=bank[i % 2][:, f, :], op0=ALU.add, op1=ALU.mult).then_inc(s_ha, 1)
                if i >= 1:
                    add_expert(i - 1)
            add_expert(E * NC - 1)
            for c in range(NC):
                dve.wait_ge(s_yload[c], 32)
                cs = slice(c * N, (c + 1) * N)
                link(dve.reciprocal(y_den[:, cs], y_den[:, cs]))
                dve.tensor_tensor(y_num[:, cs], y_num[:, cs], y_den[:, cs], ALU.mult).then_inc(s_y, 1)
            for c in range(NC):
                dve.wait_ge(s_att, c + 1)
                dst = moe[:, TPC * c:TPC * (c + 1), :]
                dve.tensor_tensor(dst, dst, flat(c).rearrange("p (n c) -> p n c", n=TPC), ALU.add).then_inc(s_out, 1)

        @block.tensor
        def _(pe):
            pe.wait_ge(s_ident, 1)
            pe.wait_ge(s_w, 48)
            for i in range(4):
                pe.transpose(flat(0)[:, i * C:(i + 1) * C], w_rows[:, i, :], ident[:, :])
            pe.transpose(flat(1)[:, 0:E], cw_rows[:, :], ident[0:E, 0:E]).then_inc(s_wt_ps, 1)
            for c in range(NC):
                pe.wait_ge(s_xn, c + 1)
                if c >= 2:
                    pe.wait_ge(s_xt, c - 1)
                for t in range(TPC):
                    last = pe.transpose(flat(6 + c % 2)[:, t * P:(t + 1) * P], xn[:, TPC * c + t, :], ident[:, :])
                last.then_inc(s_xt_ps, 1)
            pe.wait_ge(s_wt, 2)
            for c in range(NC):
                pe.wait_ge(s_xt, c + 1)
                if c >= 2:
                    pe.wait_ge(s_q, c - 1)
                    pe.wait_ge(s_k, c - 1)
                    pe.wait_ge(s_v, c - 1)
                f = 3 * (c % 2)
                for i in range(2):
                    pe.matmul(flat(f + i), wT[:, i, :], xnT[:, c * N:(c + 1) * N], start=True, stop=True)
                for t in range(TPC):
                    last = pe.matmul(flat(f + 2)[:, t * C:(t + 1) * C], xnT[:, c * N + t * P:c * N + (t + 1) * P],
                                     wT[:, 2, :], start=True, stop=True)
                last.then_inc(s_qkv_ps, 1)
            for n in range(NT):
                last = pe.matmul(flat(7)[:, n * E:(n + 1) * E], xnT[:, n * P:(n + 1) * P], cwT[:, :],
                                 start=True, stop=True)
            last.then_inc(s_logit, 1)
            pe.wait_ge(s_const, 6)
            pe.wait_ge(s_q, NC)
            pe.wait_ge(s_k, NC)
            pe.wait_ge(s_v, NC)
            for i in range(2 * NC):
                pe.wait_ge(s_sq, i + 1)
                if i == 7:
                    pe.wait_ge(s_lmax, 1)
                pe.matmul(flat(i)[0:H, :], head_sel[:, :], sq[:, :], start=True, stop=True).then_inc(s_norm, 1)
            pe.wait_ge(s_mm, NC)
            pe.wait_ge(s_lexp, 1)

            pe.wait_ge(s_flag, 1)
            loose = pe.value_load(flag[0:1, 0:1], min_val=0, max_val=1)
            with pe.If(loose > 0):
                with pe.Fori(0, G) as g:
                    pe.wait_ge(s_gstage, 16 * (HG + 2) * (g + 1))
                    for h in range(HG):
                        for n in range(NT):
                            pe.wait_ge(s_gread, HG * NT * g + h * NT + n + 1)
                            for c in range(n // TPC + 1):
                                last = pe.matmul(flat(c), q_aug[:, h, n * P:(n + 1) * P],
                                                 k_aug[:, h // 2, c * N:(c + 1) * N], start=True, stop=True)
                            last.then_inc(s_gscore, 1)

            def score(g, u):
                k, p = u // 2, u % 2
                c, j = STEPS[k]
                off = max(0, j - TPC * c) * P
                if p == 0 and j == 0:
                    pe.wait_ge(s_stage_q[c], 16 * HG * (g + 1))
                if p == 0 and j == TPC * c:
                    pe.wait_ge(s_stage_k[c], 16 * 2 * (g + 1))
                pe.wait_ge(s_exp, NU * g + SB + before(u))
                for a in range(2):
                    last = pe.matmul(scores[u % SB][:, a, off:N],
                                     k_aug[:, p, j * P:(j + 1) * P],
                                     q_aug[:, 2 * p + a, c * N + off:(c + 1) * N], start=True, stop=True)
                last.then_inc(s_sready, 1)

            def values(g, k):
                c, j = STEPS[k]
                off = max(0, j - TPC * c) * P
                if k == 0:
                    pe.wait_ge(s_vgrp, g + 1)
                if j == 0:
                    pe.wait_ge(s_accfree, NC * g + c + 1)
                if j >= TPC * c:
                    pe.wait_ge(s_mask, NT * g + j + 1)
                else:
                    pe.wait_ge(s_exp, NU * g + SB + 2 * k + 2)
                for h in range(HG):
                    last = pe.matmul(acc[32 * h:32 * h + 32, off:N], v_grp[:, j, h, :], probs[:, k % PB, h, off:N],
                                     start=(j == 0), stop=(j == TPC * (c + 1) - 1))
                last.then_inc(s_pfree, 1)

            def group(g, last):
                for k in range(NS):
                    for u in (2 * k + LEAD, 2 * k + LEAD + 1):
                        if u < NU:
                            score(g, u)
                        elif not last:
                            score(g + 1, u - NU)
                    values(g, k)

            for u in range(LEAD):
                score(0, u)
            with pe.Fori(0, G - 1) as g:
                group(g, False)
            group(G - 1, True)

            pe.wait_ge(s_eq, 1)
            pe.matmul(spare[:, 0:NT * E], tri[:, :], eq[:, :, :].rearrange("p n e -> p (n e)"), start=True, stop=True)
            pe.matmul(spare[:, NT * E:2 * NT * E], ones_pp[:, :], eq[:, :, :].rearrange("p n e -> p (n e)"),
                      start=True, stop=True)
            pe.matmul(spare[:, 2 * NT * E:2 * NT * E + E], ones_pp[:, :], gt_n[:, :], start=True, stop=True)\
              .then_inc(s_rank, 1)

            pe.wait_ge(s_moe_w, 32)

            def down(i):
                e = i // NC
                pe.wait_ge(s_ha, FH * (i + 1))
                if i >= 2:
                    pe.wait_ge(s_moread, i - 1)
                for t in range(TPC):
                    for f in range(FH):
                        last = pe.matmul(bank[2][:, i % 2, t * C:(t + 1) * C], hT[:, i % 2, f, t * P:(t + 1) * P],
                                         w2_sb[:, e, f, :], start=(f == 0), stop=(f == FH - 1))
                last.then_inc(s_mo, 1)

            for i in range(E * NC):
                e, c = i // NC, i % NC
                for f in range(FH):
                    if i >= 2:
                        pe.wait_ge(s_ha, FH * (i - 2) + f + 1)
                    pe.matmul(bank[i % 2][:, f, :], w1_sb[:, e, f * P:(f + 1) * P], xnT[:, c * N:(c + 1) * N],
                              start=True, stop=True).then_inc(s_h, 1)
                if i >= 1:
                    down(i - 1)
            down(E * NC - 1)
            for c in range(NC):
                pe.wait_ge(s_y, c + 1)
                for t in range(TPC):
                    n = TPC * c + t
                    last = pe.matmul(flat(c)[:, t * C:(t + 1) * C], y_num[:, n * P:(n + 1) * P], wT[:, 3, :],
                                     start=True, stop=True)
                last.then_inc(s_att, 1)


_INS = ['L0_attn_x', 'L0_attn_W_attn', 'L0_attn_b_attn', 'L0_attn_W_proj', 'L0_attn_b_proj', 'L0_ffn_choice_w',
        'L0_ffn_w1', 'L0_ffn_w2']


def kernel(**inputs):
    import numpy as _np
    import concourse.bacc as _bacc
    from concourse import mybir as _mybir
    from concourse.bass_utils import run_bass_kernel_spmd as _run

    nc = _bacc.Bacc("TRN2", target_bir_lowering=False, num_devices=1)
    arrays, args = {}, []
    for name in _INS:
        a = _np.ascontiguousarray(inputs[name])
        arrays[f"in_{name}_dram"] = a
        args.append(nc.dram_tensor(f"in_{name}_dram", a.shape, _mybir.dt.from_np(a.dtype), kind="ExternalInput").ap())
    shape = inputs['L0_attn_x'].shape
    args.append(nc.dram_tensor("out_0_dram", shape, _mybir.dt.float32, kind="ExternalOutput").ap())
    block_kernel(nc, *args)
    r = _run(nc, [arrays], core_ids=[0])
    return r.results[0]["out_0_dram"]
```
